# Optimizing a Trainium2 kernel written in Bass

```python
import numpy as np
import jax
import jax.numpy as jnp

def _softmax(x, axis=-1):
    return jax.nn.softmax(x, axis=axis)
def _gelu(x):
    return jax.nn.gelu(x, approximate=True)
def _silu(x):
    return jax.nn.silu(x)
def _sigmoid(x):
    return jax.nn.sigmoid(x)
def _layernorm(x, axis=-1, eps=1e-5):
    m = jnp.mean(x, axis=axis, keepdims=True)
    v = jnp.var(x, axis=axis, keepdims=True)
    return (x - m) / jnp.sqrt(v + eps)
def _scatter_add(tgt, idx, src, axis=0):
    return tgt.at[idx].add(src)
def _segment_sum(src, seg, n):
    return jax.ops.segment_sum(src, seg, n)

kernel_name = 'mk_conv_seq_d1_conv_nhwc64_785c9d'

def setup_inputs(seed: int = 0):
    np.random.seed(seed)
    _w = jnp.asarray
    def _rec_inputs():
        import jax
        import jax.numpy as jnp
        _gk = jax.random.key(seed)
        x = 0.001231 + 1 * jax.random.normal(jax.random.fold_in(_gk, 1), (2, 256, 64, 64), jnp.float32)
        return x
    x = _rec_inputs()
    def _L0_conv_setup():
        import jax, jax.numpy as jnp
        import numpy as np
        DIM = 256
        Hh = 64
        Ww = 64
        L = Hh * Ww
        Bsz = 2
        D_IN = 512
        DS = 16
        DTR = 16
        DCONV = 4

        def _layernorm(x, g, b):
            mu = jnp.mean(x, axis=-1, keepdims=True)
            var = jnp.var(x, axis=-1, keepdims=True)
            return (x - mu) * jax.lax.rsqrt(var + 1e-05) * g + b

        def _mamba(u, in_proj, conv_w, conv_b, x_proj, dt_w, dt_b, A_log, D, out_proj):
            bsz, ls, _ = u.shape
            xz = u @ in_proj
            x, z = jnp.split(xz, 2, axis=-1)
            dconv = conv_w.shape[1]
            xp = jnp.pad(x, ((0, 0), (dconv - 1, 0), (0, 0)))
            xc = conv_b + sum((xp[:, k:k + ls, :] * conv_w[:, k] for k in range(dconv)))
            x = jax.nn.silu(xc)
            x_dbl = x @ x_proj
            dtr = dt_w.shape[0]
            ds = A_log.shape[1]
            dt, Bs, Cs = jnp.split(x_dbl, [dtr, dtr + ds], axis=-1)
            delta = jax.nn.softplus(dt @ dt_w + dt_b)
            A = -jnp.exp(A_log)

            def step(h, inp):
                xt, dtt, Bt, Ct = inp
                dA = jnp.exp(dtt[:, :, None] * A)
                h = h * dA + (dtt * xt)[:, :, None] * Bt[:, None, :]
                return (h, jnp.einsum('bds,bs->bd', h, Ct))
            h0 = jnp.zeros((bsz, A.shape[0], ds), u.dtype)
            xs = (x.transpose(1, 0, 2), delta.transpose(1, 0, 2), Bs.transpose(1, 0, 2), Cs.transpose(1, 0, 2))
            _, ys = jax.lax.scan(step, h0, xs)
            y = ys.transpose(1, 0, 2) + x * D
            y = y * jax.nn.silu(z)
            return y @ out_proj
        key = jax.random.key(seed)
        ks = jax.random.split(key, 8)
        rn = lambda k, shape, s: jax.random.normal(k, shape, jnp.float32) * s
        perm = lambda k: jax.random.permutation(k, L)
        spiral_eye = jax.nn.one_hot(perm(ks[0]), L, dtype=jnp.float32)
        despiral_eye = jax.nn.one_hot(perm(ks[1]), L, dtype=jnp.float32)
        despiral_r_eye = jax.nn.one_hot(perm(ks[2]), L, dtype=jnp.float32)
        x = rn(ks[3], (Bsz, DIM, Hh, Ww), 1.0)

        def mamba_params(kb, pfx):
            kk = jax.random.split(kb, 5)
            return {pfx + '_in_proj': rn(kk[0], (DIM, 2 * D_IN), DIM ** (-0.5)), pfx + '_conv_w': rn(kk[1], (D_IN, DCONV), DCONV ** (-0.5)), pfx + '_conv_b': jnp.zeros((D_IN,), jnp.float32), pfx + '_x_proj': rn(kk[2], (D_IN, DTR + 2 * DS), D_IN ** (-0.5)), pfx + '_dt_w': rn(kk[3], (DTR, D_IN), DTR ** (-0.5)), pfx + '_dt_b': jnp.full((D_IN,), float(np.log(np.expm1(0.01))), jnp.float32), pfx + '_A_log': jnp.log(jnp.tile(jnp.arange(1, DS + 1, dtype=jnp.float32), (D_IN, 1))), pfx + '_D': jnp.ones((D_IN,), jnp.float32), pfx + '_out_proj': rn(kk[4], (D_IN, DIM), D_IN ** (-0.5))}
        inp = {'x': x, 'spiral_eye': spiral_eye, 'despiral_eye': despiral_eye, 'despiral_r_eye': despiral_r_eye, 'ln_gamma': jnp.ones((DIM,), jnp.float32), 'ln_beta': jnp.zeros((DIM,), jnp.float32)}
        inp.update(mamba_params(ks[4], 'm1'))
        inp.update(mamba_params(ks[5], 'm2'))
        inp['conv_w'] = rn(ks[6], (256, 512), 512 ** (-0.5))
        inp['conv_b'] = jnp.zeros((256,), jnp.float32)
        return inp
    _L0_conv_all = _L0_conv_setup()
    _L0_conv_in = {k: v for k, v in _L0_conv_all.items() if k in ('spiral_eye', 'despiral_eye', 'despiral_r_eye', 'ln_gamma', 'ln_beta', 'm1_in_proj', 'm1_conv_w', 'm1_conv_b', 'm1_x_proj', 'm1_dt_w', 'm1_dt_b', 'm1_A_log', 'm1_D', 'm1_out_proj', 'm2_in_proj', 'm2_conv_w', 'm2_conv_b', 'm2_x_proj', 'm2_dt_w', 'm2_dt_b', 'm2_A_log', 'm2_D', 'm2_out_proj', 'conv_w', 'conv_b', )}
    del _L0_conv_all

    return {
        "x": x,
        "L0_conv_spiral_eye": _L0_conv_in["spiral_eye"],
        "L0_conv_despiral_eye": _L0_conv_in["despiral_eye"],
        "L0_conv_despiral_r_eye": _L0_conv_in["despiral_r_eye"],
        "L0_conv_ln_gamma": _L0_conv_in["ln_gamma"],
        "L0_conv_ln_beta": _L0_conv_in["ln_beta"],
        "L0_conv_m1_in_proj": _L0_conv_in["m1_in_proj"],
        "L0_conv_m1_conv_w": _L0_conv_in["m1_conv_w"],
        "L0_conv_m1_conv_b": _L0_conv_in["m1_conv_b"],
        "L0_conv_m1_x_proj": _L0_conv_in["m1_x_proj"],
        "L0_conv_m1_dt_w": _L0_conv_in["m1_dt_w"],
        "L0_conv_m1_dt_b": _L0_conv_in["m1_dt_b"],
        "L0_conv_m1_A_log": _L0_conv_in["m1_A_log"],
        "L0_conv_m1_D": _L0_conv_in["m1_D"],
        "L0_conv_m1_out_proj": _L0_conv_in["m1_out_proj"],
        "L0_conv_m2_in_proj": _L0_conv_in["m2_in_proj"],
        "L0_conv_m2_conv_w": _L0_conv_in["m2_conv_w"],
        "L0_conv_m2_conv_b": _L0_conv_in["m2_conv_b"],
        "L0_conv_m2_x_proj": _L0_conv_in["m2_x_proj"],
        "L0_conv_m2_dt_w": _L0_conv_in["m2_dt_w"],
        "L0_conv_m2_dt_b": _L0_conv_in["m2_dt_b"],
        "L0_conv_m2_A_log": _L0_conv_in["m2_A_log"],
        "L0_conv_m2_D": _L0_conv_in["m2_D"],
        "L0_conv_m2_out_proj": _L0_conv_in["m2_out_proj"],
        "L0_conv_conv_w": _L0_conv_in["conv_w"],
        "L0_conv_conv_b": _L0_conv_in["conv_b"],
    }

def reference(x, L0_conv_spiral_eye, L0_conv_despiral_eye, L0_conv_despiral_r_eye, L0_conv_ln_gamma, L0_conv_ln_beta, L0_conv_m1_in_proj, L0_conv_m1_conv_w, L0_conv_m1_conv_b, L0_conv_m1_x_proj, L0_conv_m1_dt_w, L0_conv_m1_dt_b, L0_conv_m1_A_log, L0_conv_m1_D, L0_conv_m1_out_proj, L0_conv_m2_in_proj, L0_conv_m2_conv_w, L0_conv_m2_conv_b, L0_conv_m2_x_proj, L0_conv_m2_dt_w, L0_conv_m2_dt_b, L0_conv_m2_A_log, L0_conv_m2_D, L0_conv_m2_out_proj, L0_conv_conv_w, L0_conv_conv_b):
    import jax
    import jax.numpy as jnp
    def _L0_conv_ref(x, spiral_eye, despiral_eye, despiral_r_eye, ln_gamma, ln_beta, m1_in_proj, m1_conv_w, m1_conv_b, m1_x_proj, m1_dt_w, m1_dt_b, m1_A_log, m1_D, m1_out_proj, m2_in_proj, m2_conv_w, m2_conv_b, m2_x_proj, m2_dt_w, m2_dt_b, m2_A_log, m2_D, m2_out_proj, conv_w, conv_b):
        import jax, jax.numpy as jnp
        import numpy as np
        DIM = 256
        Hh = 64
        Ww = 64
        L = Hh * Ww
        Bsz = 2
        D_IN = 512
        DS = 16
        DTR = 16
        DCONV = 4

        def _layernorm(x, g, b):
            mu = jnp.mean(x, axis=-1, keepdims=True)
            var = jnp.var(x, axis=-1, keepdims=True)
            return (x - mu) * jax.lax.rsqrt(var + 1e-05) * g + b

        def _mamba(u, in_proj, conv_w, conv_b, x_proj, dt_w, dt_b, A_log, D, out_proj):
            bsz, ls, _ = u.shape
            xz = u @ in_proj
            x, z = jnp.split(xz, 2, axis=-1)
            dconv = conv_w.shape[1]
            xp = jnp.pad(x, ((0, 0), (dconv - 1, 0), (0, 0)))
            xc = conv_b + sum((xp[:, k:k + ls, :] * conv_w[:, k] for k in range(dconv)))
            x = jax.nn.silu(xc)
            x_dbl = x @ x_proj
            dtr = dt_w.shape[0]
            ds = A_log.shape[1]
            dt, Bs, Cs = jnp.split(x_dbl, [dtr, dtr + ds], axis=-1)
            delta = jax.nn.softplus(dt @ dt_w + dt_b)
            A = -jnp.exp(A_log)

            def step(h, inp):
                xt, dtt, Bt, Ct = inp
                dA = jnp.exp(dtt[:, :, None] * A)
                h = h * dA + (dtt * xt)[:, :, None] * Bt[:, None, :]
                return (h, jnp.einsum('bds,bs->bd', h, Ct))
            h0 = jnp.zeros((bsz, A.shape[0], ds), u.dtype)
            xs = (x.transpose(1, 0, 2), delta.transpose(1, 0, 2), Bs.transpose(1, 0, 2), Cs.transpose(1, 0, 2))
            _, ys = jax.lax.scan(step, h0, xs)
            y = ys.transpose(1, 0, 2) + x * D
            y = y * jax.nn.silu(z)
            return y @ out_proj
        B, C, H, W = x.shape
        x1 = x.reshape(B, C, H * W)
        x1 = jnp.einsum('ij,bcj->bci', spiral_eye, x1).transpose(0, 2, 1)
        x2 = jnp.flip(x1, axis=1)
        m1 = _mamba(_layernorm(x1, ln_gamma, ln_beta), m1_in_proj, m1_conv_w, m1_conv_b, m1_x_proj, m1_dt_w, m1_dt_b, m1_A_log, m1_D, m1_out_proj)
        m2 = _mamba(_layernorm(x2, ln_gamma, ln_beta), m2_in_proj, m2_conv_w, m2_conv_b, m2_x_proj, m2_dt_w, m2_dt_b, m2_A_log, m2_D, m2_out_proj)
        out1 = jnp.einsum('ij,bcj->bci', despiral_eye, m1.transpose(0, 2, 1)).reshape(B, C, H, W)
        out2 = jnp.einsum('ij,bcj->bci', despiral_r_eye, m2.transpose(0, 2, 1)).reshape(B, C, H, W)
        cat = jnp.concatenate([out1, out2], axis=1)
        out = jnp.einsum('oc,bchw->bohw', conv_w, cat) + conv_b[None, :, None, None]
        return out.reshape(-1, 256, 64, 64)

    def _gn(v, G=32, eps=1e-5):
        B_, H_, W_, C_ = v.shape
        g = v.reshape(B_, H_, W_, G, C_ // G)
        m = jnp.mean(g, axis=(1, 2, 4), keepdims=True)
        s = jnp.var(g, axis=(1, 2, 4), keepdims=True)
        return ((g - m) / jnp.sqrt(s + eps)).reshape(v.shape)

    def _ln_c(v, eps=1e-6):
        m = jnp.mean(v, axis=-1, keepdims=True)
        s = jnp.var(v, axis=-1, keepdims=True)
        return (v - m) / jnp.sqrt(s + eps)

    def _ln_t(v, eps=1e-5):
        m = jnp.mean(v, axis=-1, keepdims=True)
        s = jnp.var(v, axis=-1, keepdims=True)
        return (v - m) / jnp.sqrt(s + eps)

    def _to_tokens(v):
        B_, H_, W_, C_ = v.shape
        return v.reshape(B_, H_ * W_, C_)
    def _from_tokens(t, like):
        return t.reshape(like.shape)

    x = _L0_conv_ref(x, L0_conv_spiral_eye, L0_conv_despiral_eye, L0_conv_despiral_r_eye, L0_conv_ln_gamma, L0_conv_ln_beta, L0_conv_m1_in_proj, L0_conv_m1_conv_w, L0_conv_m1_conv_b, L0_conv_m1_x_proj, L0_conv_m1_dt_w, L0_conv_m1_dt_b, L0_conv_m1_A_log, L0_conv_m1_D, L0_conv_m1_out_proj, L0_conv_m2_in_proj, L0_conv_m2_conv_w, L0_conv_m2_conv_b, L0_conv_m2_x_proj, L0_conv_m2_dt_w, L0_conv_m2_dt_b, L0_conv_m2_A_log, L0_conv_m2_D, L0_conv_m2_out_proj, L0_conv_conv_w, L0_conv_conv_b)
    return x


_drawn_inputs = setup_inputs


def setup_inputs(seed=0):
    import zlib

    import numpy as np

    out = dict(_drawn_inputs(seed))
    spreads = {'L0_conv_ln_gamma': (1.0, 0.2),
     'L0_conv_ln_beta': (0.0, 0.1),
     'L0_conv_m1_conv_b': (0.0, 0.1),
     'L0_conv_m1_dt_b': (-4.600165843963623, 0.2),
     'L0_conv_m1_D': (1.0, 0.2),
     'L0_conv_m2_conv_b': (0.0, 0.1),
     'L0_conv_m2_dt_b': (-4.600165843963623, 0.2),
     'L0_conv_m2_D': (1.0, 0.2),
     'L0_conv_conv_b': (0.0, 0.1)}
    factors = {}
    for name, (base, spread) in spreads.items():
        noise = np.random.default_rng([zlib.crc32(name.encode()), seed]).standard_normal(out[name].shape)
        drawn = base * np.exp(spread * noise) if base else spread * noise
        out[name] = jnp.asarray(drawn.astype(out[name].dtype))
    for name, factor in factors.items():
        out[name] = (out[name] * factor).astype(out[name].dtype)
    return out
```

```python
from contextlib import ExitStack

import concourse.bass as bass
from concourse import mybir

F32 = mybir.dt.float32
BF16 = mybir.dt.bfloat16
ALU = mybir.AluOpType
ACT = mybir.ActivationFunctionType

P = 128
BATCH, DIM, L = 2, 256, 4096
DIN, DS, DTR, TAPS = 512, 16, 16, 4
T = 512
NCH = L // T
KD = DIM // P
KI = DIN // P
NT = L // P
BC = BATCH * DIM
UNITS = NCH * BATCH
EPS = 1e-5
SP_CLIP = 40.0
SLOTS = UNITS + 1

FRONT_STEPS = {0: ["x0"], 1: ["x1"], 2: ["x2"], 3: ["x3"], 4: ["c0"], 5: ["c1", "z0"], 6: ["c2", "z1"],
               7: ["c3", "z2"], 8: ["z3"], 9: ["proj"], 10: ["d0", "d1"], 11: ["d2", "d3"]}
OUT_STEPS = {2: ["t0", "t1"], 3: ["t2", "t3"], 12: ["o0"], 13: ["o1"]}


def step_products(s):
    ahead = s + 2
    broadcasts = [("B", ahead), ("C", ahead)]
    return broadcasts + [(p, None) for p in FRONT_STEPS.get(s, []) + OUT_STEPS.get(s, [])]


UNIT_PRODUCTS = [p for s in range(DS) for p in step_products(s)]
FIRST_FRONT = [(p, None) for s in sorted(FRONT_STEPS) for p in FRONT_STEPS[s]] + [
    ("B", DS), ("C", DS), ("B", DS + 1), ("C", DS + 1)]
TAIL = [(p, None) for s in sorted(OUT_STEPS) for p in OUT_STEPS[s]]
AT = {p[0] + (str(p[1]) if p[1] is not None else ""): i for i, p in enumerate(UNIT_PRODUCTS)}
NU, NF, NTAIL, NW2 = len(UNIT_PRODUCTS), len(FIRST_FRONT), len(TAIL), KI
DIR_PRODUCTS = NW2 + NF + UNITS * NU + NTAIL
LAG = 2
RING = 4
DIR_SUMS = RING + LAG + UNITS * DS
GRAB = (1, 1, 0, 9)
MAKE = (2, 0, 9, 0)
ROWS = T + L
MARK = 8192
FRONTS = UNITS + 1


def build(nc, t):
    with ExitStack() as ctx:
        def sem(name):
            return ctx.enter_context(nc.semaphore(name))

        def psum(name, shape):
            return ctx.enter_context(nc.psum_tensor(name, shape, F32))

        y_ps = psum("y_ps", [P, KI, T])
        da_ps = psum("da_ps", [P, 2, T])
        g_ps = psum("g_ps", [P, 2, T])
        words = 50 * 1024
        arena = ctx.enter_context(nc.sbuf_tensor("arena", [P, words], F32))
        xt_scr = nc.dram_tensor("xt_scr", (2 * NCH + 1, BATCH, P, KD * T), F32).ap()
        tok_scr = nc.dram_tensor("tok_scr", (2 * ROWS, BC), F32).ap()
        rows = ctx.enter_context(nc.sbuf_tensor("rows", [P, 3 * NT], mybir.dt.int32))
        perm = ctx.enter_context(nc.sbuf_tensor("perm", [1, 2], mybir.dt.int32))
        find_rows(nc, t, arena, y_ps, rows, perm, sem)
        prologue(nc, t, arena, y_ps, g_ps, xt_scr, rows, perm, sem)
        scan_phase(nc, t, arena, y_ps, da_ps, g_ps, xt_scr, tok_scr, sem)
        epilogue(nc, t, arena, y_ps, tok_scr, rows, perm, sem)


def find_rows(nc, t, arena, y_ps, rows, perm, sem):
    c = Carve(arena)
    NB = 4
    N = 3 * NT
    iota = c.take(L)
    eye = c.take(NB * L).rearrange("p (i n) -> p i n", i=NB)
    marked = c.take(2 * L).rearrange("p (i n) -> p i n", i=2)
    copied = c.take(2 * L).rearrange("p (i n) -> p i n", i=2)
    mark, total = c.take(N), c.take(N)
    good = c.take(N)
    count = c.take(2)
    ones = c.take(1)
    iota_ld, eye_ld = sem("iota_ld"), [sem(f"eye_ld{i}") for i in range(NB)]
    mark_done, total_done, chain, counted = sem("mark_done"), sem("total_done"), sem("chain"), sem("counted")

    with nc.Block() as block:
        @block.sync
        def _(sp):
            sp.dma_start(iota, t["iota"].to_broadcast([P, L])).then_inc(iota_ld, 16)
            for q in range(NB):
                sp.dma_start(eye[:, q], t["eyes"][q]).then_inc(eye_ld[q], 16)
            with sp.Fori(0, N // NB - 1) as i:
                for q in range(NB):
                    nxt = sp.snap(i * NB + NB + q)
                    sp.wait_ge(mark_done, i * NB + (q + 3))
                    sp.wait_ge(total_done, i * NB + (q + 3))
                    sp.dma_start(eye[:, q], t["eyes"][nxt]).then_inc(eye_ld[q], 16)

        @block.vector
        def _(dve):
            nc.vector.memset(ones, 1.0).then_inc(mark_done, 2)
            nc.vector.memset(good, 0.0).then_inc(total_done, 2)
            nc.vector.memset(mark, 0.0).then_inc(chain, 1)
            nc.vector.memset(total, 0.0).then_inc(chain, 1)
            dve.wait_ge(chain, 2)
            with dve.Fori(0, N // NB) as i:
                for q in range(NB):
                    dve.wait_ge(eye_ld[q], i * 16 + 16)
                    dve.wait_ge(mark_done, i * NB + (q + 1))
                    dve.wait_ge(iota_ld, 16)
                    nc.vector.scalar_tensor_tensor(marked[:, q % 2], eye[:, q], 0.0, iota, ALU.not_equal, ALU.mult,
                                                   accum_out=mark[:, bass.ds(i * NB + q, 1)]).then_inc(mark_done, 1)
            steps = [0]

            def link(ins):
                steps[0] += 1
                ins.then_inc(chain, 1)
                dve.wait_ge(chain, steps[0] + 2)

            dve.wait_ge(mark_done, N + 2)
            dve.wait_ge(total_done, N + 2)
            link(nc.vector.tensor_scalar(good, mark, float(MARK), None, ALU.is_ge))
            link(nc.vector.scalar_tensor_tensor(good, mark, 2.0 * MARK, good, ALU.is_lt, ALU.mult))
            link(nc.vector.scalar_tensor_tensor(good, total, 1.0, good, ALU.is_equal, ALU.mult))
            link(nc.vector.reduce_sum(count[:, 0:1], good[:, 0:NT], mybir.AxisListType.X))
            link(nc.vector.reduce_sum(count[:, 1:2], good[:, NT:N], mybir.AxisListType.X))
            for m, base in enumerate((0, T, ROWS + T)):
                nc.vector.tensor_scalar(rows[:, m * NT:(m + 1) * NT], mark[:, m * NT:(m + 1) * NT],
                                        float(base - MARK), None, ALU.add)
            dve.wait_ge(counted, 1)
            for m, n in enumerate((L, 2 * L)):
                nc.vector.tensor_scalar(perm[:, m:m + 1], y_ps[0:1, 0, m:m + 1], float(n), None, ALU.is_equal)

        @block.scalar
        def _(act):
            act.wait_ge(chain, 2)
            with act.Fori(0, N // NB) as i:
                for q in range(NB):
                    act.wait_ge(eye_ld[q], i * 16 + 16)
                    act.wait_ge(total_done, i * NB + (q + 1))
                    act.wait_ge(iota_ld, 16)
                    nc.scalar.activation(copied[:, q % 2], eye[:, q], ACT.Copy,
                                         accum_out=total[:, bass.ds(i * NB + q, 1)]).then_inc(total_done, 1)

        @block.tensor
        def _(pe):
            pe.wait_ge(chain, 2 + 5)
            nc.tensor.matmul(y_ps[0:1, 0, 0:2], ones, count, start=True, stop=True).then_inc(counted, 1)


class Carve:

    def __init__(self, arena):
        self.arena, self.at = arena, 0

    def take(self, n):
        a = self.arena[:, self.at:self.at + n]
        self.at += n
        assert self.at <= self.arena.shape[1]
        return a


def prologue(nc, t, arena, y_ps, g_ps, xt_scr, rows, perm, sem):
    c = Carve(arena)
    ident = c.take(P)
    rev = c.take(P)
    gb = c.take(2 * KD)
    eps = c.take(1)
    hold = c.take(4)
    stats = c.take(2 * BATCH * 6).rearrange("p (i b k) -> p i b k", i=2, b=BATCH)
    mv = c.take(2 * BATCH * 2).rearrange("p (i b k) -> p i b k", i=2, b=BATCH)
    lnv = c.take(2 * BATCH).rearrange("p (i b k) -> p i b k", i=2, b=BATCH)
    rstd = c.take(2 * BATCH).rearrange("p (i b) -> p i b", i=2)
    x_sb = c.take(NT * BC).rearrange("p (j n) -> p j n", j=NT)
    s_sb = c.take(2 * NT * P).rearrange("p (i j n) -> p i j n", i=2, j=NT)
    xn = c.take(2 * BC).rearrange("p (i n) -> p i n", i=2)
    x_tok = c.take(2 * BC).rearrange("p (i n) -> p i n", i=2)
    xtf = c.take(BATCH * KD * T).rearrange("p (b h n) -> p b h n", b=BATCH, h=KD)
    xtr = c.take(BATCH * KD * T).rearrange("p (b h n) -> p b h n", b=BATCH, h=KD)
    TC = T // P

    const_ld, x_ld, s_ld0, s_ld1 = sem("const_ld"), sem("x_ld"), sem("s_ld0"), sem("s_ld1")
    s_ld = [s_ld0, s_ld1]
    x_got = [sem("x_got0"), sem("x_got1")]
    eps_set, acc_done, stat_done, mv_done = sem("eps_set"), sem("acc_done"), sem("stat_done"), sem("mv_done")
    ln_done, rstd_done, xn_done = sem("ln_done"), sem("rstd_done"), sem("xn_done")
    tr_done, tr_used, xt_out = sem("tr_done"), sem("tr_used"), sem("xt_out")

    with nc.Block() as block:
        @block.sync
        def _(sp):
            sp.dma_start(ident, t["ident"]).then_inc(const_ld, 16)
            sp.dma_start(rev, t["rev"]).then_inc(const_ld, 16)
            sp.dma_start(gb, t["ln"]).then_inc(const_ld, 16)
            def store(ch, back):
                sp.wait_ge(tr_used, ch * (4 * TC) + (4 * TC + 5))
                sp.dma_start(xt_scr[ch].rearrange("b p n -> p b n"),
                             xtf.rearrange("p b h n -> p b (h n)")).then_inc(xt_out, 16)
                sp.dma_start(xt_scr[back].rearrange("b p n -> p b n"),
                             xtr.rearrange("p b h n -> p b (h n)")).then_inc(xt_out, 16)

            for b in range(BATCH):
                sp.dma_start(xt_scr[2 * NCH, b], t["x"][:, 0:2].rearrange("p j n -> p (j n)")).then_inc(xt_out, 16)
            gathered = sp.value_load(perm[0:1, 0:1], min_val=0, max_val=1)
            with sp.If(gathered == 1):
                with sp.Fori(0, NCH) as ch:
                    back = sp.snap(2 * NCH - 1 - ch)
                    store(ch, back)
            with sp.Else():
                for q in range(4):
                    n = NT // 4
                    sp.dma_start(x_sb[:, q * n:(q + 1) * n], t["x"][:, q * n:(q + 1) * n, :]).then_inc(x_ld, 16)
                    if q < 2:
                        sp.dma_start(s_sb[:, q], t["spiral"][q]).then_inc(s_ld[q], 16)
                with sp.Fori(0, NCH) as ch:
                    back = sp.snap(2 * NCH - 1 - ch)
                    for q in range(TC):
                        nxt = sp.snap(ch * TC + (q + 2))
                        sp.wait_ge(acc_done, ch * TC + (q + 1))
                        sp.dma_start(s_sb[:, q % 2], t["spiral"][nxt]).then_inc(s_ld[q % 2], 16)
                    store(ch, back)
                sp.wait_ge(s_ld[0], 16 * (NT // 2 + 1))
                sp.wait_ge(s_ld[1], 16 * (NT // 2 + 1))
            sp.wait_ge(xt_out, 32 * (NCH + 1))

        @block.tensor
        def _(pe):
            def normed_transposes(tile, ch, q):
                pe.wait_ge(xn_done, tile + 1)
                pe.wait_ge(tr_used, tile * 4 - 3)
                for i in range(BATCH * KD):
                    nc.tensor.transpose(g_ps[:, 0, i * P:(i + 1) * P], xn[:, q % 2, i * P:(i + 1) * P], ident)
                for i in range(BATCH * KD):
                    m = nc.tensor.matmul(g_ps[:, 1, i * P:(i + 1) * P], xn[:, q % 2, i * P:(i + 1) * P], rev,
                                         start=True, stop=True)
                m.then_inc(tr_done, 1)

            pe.wait_ge(const_ld, 48)
            gathered = pe.value_load(perm[0:1, 0:1], min_val=0, max_val=1)
            with pe.If(gathered == 1):
                with pe.Fori(0, NCH) as ch:
                    for q in range(TC):
                        normed_transposes(ch * TC + q + 2, ch, q)
            with pe.Else():
                pe.wait_ge(x_ld, 64)
                with pe.Fori(0, NCH) as ch:
                    for q in range(TC):
                        pe.wait_ge(s_ld[q % 2], ch * (16 * TC // 2) + 16 * (q // 2 + 1))
                        pe.wait_ge(xn_done, ch * TC + (q + 1))
                        for j in range(NT):
                            m = nc.tensor.matmul(y_ps[:, q % 2, :], s_sb[:, q % 2, j], x_sb[:, j],
                                                 start=(j == 0), stop=(j == NT - 1))
                        m.then_inc(acc_done, 1)
                        if q > 0:
                            normed_transposes(ch * TC + (q - 1) + 2, ch, q - 1)
                    normed_transposes(ch * TC + (TC - 1) + 2, ch, TC - 1)

        @block.vector
        def _(dve):
            nc.vector.memset(eps, EPS).then_inc(eps_set, 1)
            nc.vector.memset(xn[:, :, :], 0.0).then_inc(xn_done, 2)
            nc.vector.memset(hold[:, 0:1], 0.0).then_inc(tr_used, 5)
            nc.vector.memset(hold[:, 1:2], 0.0).then_inc(tr_done, 2)

            def normalise(src, arrived):
                with dve.Fori(0, NCH) as ch:
                    for q in range(TC):
                        i = q % 2
                        arrived(ch, q)
                        for b in range(BATCH):
                            st = nc.vector.bn_stats(stats[:, i, b], src[:, i, b * DIM:(b + 1) * DIM])
                        st.then_inc(stat_done, 1)
                        dve.wait_ge(stat_done, ch * TC + (q + 1))
                        nc.vector.memset(hold[:, q:q + 1], 0.0)
                        for b in range(BATCH):
                            st = nc.vector.bn_aggr(mv[:, i, b], stats[:, i, b])
                        st.then_inc(mv_done, 1)
                        dve.wait_ge(rstd_done, ch * TC + (q + 1))
                        dve.wait_ge(mv_done, ch * TC + (q + 1))
                        dve.wait_ge(tr_done, ch * TC + (q + 1))
                        for b in range(BATCH):
                            cols = slice(b * DIM, (b + 1) * DIM)
                            st = nc.vector.tensor_scalar(xn[:, i, cols], src[:, i, cols], mv[:, i, b, 0:1],
                                                         rstd[:, i, b:b + 1], ALU.subtract, ALU.mult)
                        st.then_inc(xn_done, 1)

            gathered = dve.value_load(perm[0:1, 0:1], min_val=0, max_val=1)
            with dve.If(gathered == 1):
                normalise(x_tok, lambda ch, q: dve.wait_ge(x_got[q % 2], ch * 32 + 16 * (q // 2 + 1)))
            with dve.Else():
                normalise(y_ps, lambda ch, q: dve.wait_ge(acc_done, ch * TC + (q + 1)))

        @block.scalar
        def _(act):
            act.wait_ge(const_ld, 48)
            act.wait_ge(eps_set, 1)
            nc.scalar.preload_act_table_set("natural_log_exp_and_others")
            with act.Fori(0, NCH) as ch:
                def take_transposes(q):
                    act.wait_ge(tr_done, ch * TC + (q + 3))
                    if q == 0:
                        act.wait_ge(xt_out, ch * 32 + 32)
                    for h in range(KD):
                        for bank, dst, at in ((0, xtf, q), (1, xtr, TC - 1 - q)):
                            src = g_ps[:, bank, :].rearrange("p (b h n) -> p b h n", b=BATCH, h=KD)[:, :, h]
                            nc.scalar.activation(dst[:, :, h, at * P:(at + 1) * P], src, ACT.Identity,
                                                 bias=gb[:, KD + h:KD + h + 1], scale=gb[:, h:h + 1]).then_inc(tr_used, 1)

                for q in range(TC):
                    i = q % 2
                    act.wait_ge(mv_done, ch * TC + (q + 1))
                    nc.scalar.activation(lnv[:, i], mv[:, i, :, 1:2], ACT.Ln, bias=eps).then_inc(ln_done, 1)
                    act.wait_ge(ln_done, ch * TC + (q + 1))
                    nc.scalar.activation(rstd[:, i], lnv[:, i, :, 0], ACT.Exp, scale=-0.5).then_inc(rstd_done, 1)
                    if q > 0:
                        take_transposes(q - 1)
                take_transposes(TC - 1)

        @block.gpsimd
        def _(pool):
            gathered = pool.value_load(perm[0:1, 0:1], min_val=0, max_val=1)
            with pool.If(gathered == 1):
                for i in range(NT):
                    pool.wait_ge(xn_done, i + 1)
                    pool.indirect_dma_start(x_tok[:, i % 2], None, t["x_tok"],
                                            bass.IndirectOffsetOnAxis(ap=rows[:, i:i + 1], axis=0)
                                            ).then_inc(x_got[i % 2], 16)


def scan_phase(nc, t, arena, y_ps, da_ps, g_ps, xt_scr, tok_scr, sem):
    c = Carve(arena)
    ident = c.take(P)
    clip = c.take(1)
    hold = c.take(8)
    sel = c.take(2 * DS * P // 2).bitcast(BF16).rearrange("p (s n) -> p s n", s=2 * DS)
    w_in = c.take(KD * 2 * DIN).rearrange("p (k n) -> p k n", k=KD)
    small = c.take(KI * (TAPS + 1 + 1 + 1 + DS))
    conv_w = small[:, 0:KI * TAPS].rearrange("p (k a) -> p k a", k=KI)
    conv_b = small[:, KI * TAPS:KI * (TAPS + 1)]
    dt_b = small[:, KI * (TAPS + 1):KI * (TAPS + 2)]
    d_skip = small[:, KI * (TAPS + 2):KI * (TAPS + 3)]
    a_log = small[:, KI * (TAPS + 3):]
    a_exp = c.take(KI * DS)
    a_neg = c.take(KI * DS).rearrange("p (k s) -> p k s", k=KI)
    conv_diag = c.take(KI * TAPS * P).rearrange("p (k a n) -> p k a n", k=KI, a=TAPS)
    skip_diag = c.take(KI * P).rearrange("p (k n) -> p k n", k=KI)
    w_proj = c.take(KI * P).rearrange("p (k n) -> p k n", k=KI)
    w_dt = c.take(DIN)
    w_out = c.take(KI * DIM).rearrange("p (k n) -> p k n", k=KI)
    x_in = [c.take(KD * T).rearrange("p (k n) -> p k n", k=KD) for _ in range(BATCH)]
    PAD = TAPS - 1
    x_pre = [c.take(KI * (T + PAD)).rearrange("p (k n) -> p k n", k=KI) for _ in range(BATCH)]
    xs = c.take(KI * T).rearrange("p (k n) -> p k n", k=KI)
    zs = [c.take(KI * T).rearrange("p (k n) -> p k n", k=KI) for _ in range(BATCH)]
    dt_x = c.take(KI * T).rearrange("p (k n) -> p k n", k=KI)
    y_tok = dt_x
    delta = [c.take(KI * T).rearrange("p (k n) -> p k n", k=KI) for _ in range(BATCH)]
    u = [c.take(KI * T).rearrange("p (k n) -> p k n", k=KI) for _ in range(BATCH)]
    hb = [c.take(KI * T).rearrange("p (k n) -> p k n", k=KI) for _ in range(RING)]
    b_bc = [c.take(T) for _ in range(RING)]
    c_bc = [c.take(T) for _ in range(RING)]
    proj = c.take(T)
    rest = c.take(T)
    parts = [c.take(T // 2).bitcast(BF16) for _ in range(BATCH)]
    yg = c.take(KI * T).rearrange("p (k n) -> p k n", k=KI)
    res = c.take(KI * DIM).rearrange("p (q n) -> p q n", q=KI)
    state = [c.take(DS * KI).rearrange("p (s k) -> p s k", s=DS) for _ in range(BATCH)]
    op_t = hb[0].rearrange("p k n -> p (k n)")[:, 0:KD * DIN].rearrange("p (k n) -> p k n", k=KD)
    cw_t = hb[1].rearrange("p k n -> p (k n)")[:, 0:KD * DIM].rearrange("p (k n) -> p k n", k=KD)
    W = 2 * DS

    sel_ld, w_ld, w_zero, w_ready = sem("sel_ld"), sem("w_ld"), sem("w_zero"), sem("w_ready")
    a_exped, x_ld = sem("a_exped"), [sem("xin_ld0"), sem("xin_ld1")]
    made, taken = sem("made"), sem("taken")
    silu_done, split_act, split_dve = sem("silu_done"), sem("split_act"), sem("split_dve")
    soft, delta_ready, u_ready = sem("soft"), sem("delta_ready"), sem("u_ready")
    bu_ready, da_ready, scanned = sem("bu_ready"), sem("da_ready"), sem("scanned")
    saved, hc_half, summed, gated = sem("saved"), sem("hc_half"), sem("summed"), sem("gated")
    res_out, empty_out, y_out = sem("res_out"), sem("empty_out"), sem("y_out")

    with nc.Block() as block:
        def token_rows(at, b):
            return tok_scr[bass.ds(at, T), b * DIM:(b + 1) * DIM].rearrange("(q p) n -> p q n", p=P)

        @block.sync
        def _(sp):
            sp.dma_start(ident, t["ident"]).then_inc(sel_ld, 16)
            sp.dma_start(sel[0:3 * W], t["sel"]).then_inc(sel_ld, 16)
            for d in range(2):
                sp.dma_start(tok_scr[d * ROWS:d * ROWS + T, 0:DIM], t["x_tok"][0:T, 0:DIM]).then_inc(empty_out, 16)
            with sp.Fori(0, 2) as d:
                sp.wait_ge(w_zero, 1)
                sp.wait_ge(taken, d * DIR_PRODUCTS + 1)
                sp.dma_start(w_in, t["in_proj"][d]).then_inc(w_ld, 16)
                sp.dma_start(small, t["small"][d]).then_inc(w_ld, 16)
                for r in range(3):
                    sp.dma_start(w_proj[:, :, r * W:(r + 1) * W], t["x_proj"][d][:, :, DTR:]).then_inc(w_ld, 16)
                sp.dma_start(w_proj[:, :, 3 * W:3 * W + DTR], t["x_proj"][d][:, :, 0:DTR]).then_inc(w_ld, 16)
                sp.dma_start(w_dt[3 * W:3 * W + DTR], t["dt_w"][d]).then_inc(w_ld, 16)
                sp.dma_start(op_t, t["out_proj"][d]).then_inc(w_ld, 16)
                sp.dma_start(cw_t, t["conv_w"][d]).then_inc(w_ld, 16)
                src = sp.snap(d * NCH)
                for b in range(BATCH):
                    sp.dma_start(x_in[b], xt_scr[src, b].rearrange("p (k n) -> p k n", k=KD)).then_inc(x_ld[b], 16)
                with sp.Fori(0, NCH) as ch:
                    for b in range(BATCH):
                        row = sp.snap(d * NCH + ch + 1)
                        to = sp.snap(d * ROWS + ch * T + b * T)
                        before = d * DIR_PRODUCTS + ch * (2 * NU) + (NW2 + NF + b * NU)
                        sp.wait_ge(taken, before + 1)
                        sp.dma_start(x_in[b], xt_scr[row, b].rearrange("p (k n) -> p k n", k=KD)).then_inc(x_ld[b], 16)
                        sp.wait_ge(taken, before + (AT["o1"] + 2))
                        sp.dma_start(token_rows(to, 1 - b), res).then_inc(res_out, 16)
                to = sp.snap(d * ROWS + L)
                sp.wait_ge(taken, d * DIR_PRODUCTS + DIR_PRODUCTS + 1)
                sp.dma_start(token_rows(to, 1), res).then_inc(res_out, 16)
            sp.wait_ge(empty_out, 32)
            sp.wait_ge(res_out, 16 * (2 * SLOTS) + 16)

        def product(kind, arg, at):
            return g_ps[:, at % 2]

        @block.tensor
        def _(pe):
            def make(kind, s, at, base, fb, n_front, n_unit, ob):
                bank = product(kind, s, at)
                pe.wait_ge(taken, base + (at if at else 1))
                if kind in "BC":
                    nb = fb if s >= DS else ob
                    if s == DS and kind == "B":
                        pe.wait_ge(split_act, n_front * 3 + 3)
                    row = s % DS + (DS if kind == "C" else 0)
                    m = nc.tensor.matmul(bank, sel[0:3 * W, row], parts[nb][0:3 * W], start=True, stop=True)
                elif kind[0] in "xz":
                    j = int(kind[1])
                    if kind == "x0":
                        pe.wait_ge(x_ld[fb], loads[0])
                    col = (j + (KI if kind[0] == "z" else 0)) * P
                    for k in range(KD):
                        m = nc.tensor.matmul(bank, w_in[:, k, col:col + P], x_in[fb][:, k], start=(k == 0), stop=(k == KD - 1))
                elif kind[0] == "c":
                    j = int(kind[1])
                    for a in range(TAPS):
                        m = nc.tensor.matmul(bank, conv_diag[:, j, a], x_pre[fb][:, j, a:a + T],
                                             start=(a == 0), stop=(a == TAPS - 1))
                elif kind == "proj":
                    pe.wait_ge(silu_done, n_front * 2 + 2)
                    for k in range(KI):
                        m = nc.tensor.matmul(bank, w_proj[:, k], xs[:, k], start=(k == 0), stop=(k == KI - 1))
                elif kind[0] == "d":
                    j = int(kind[1])
                    if j == 0:
                        pe.wait_ge(taken, base + (proj_at[0] + 2))
                    m = nc.tensor.matmul(bank, w_dt[3 * W:3 * W + DTR, j * P:(j + 1) * P], proj[3 * W:3 * W + DTR],
                                         start=True, stop=True)
                elif kind[0] == "t":
                    j = int(kind[1])
                    pe.wait_ge(y_out, n_unit - 1)
                    for q in range(T // P):
                        m = nc.tensor.transpose(bank[:, q * P:(q + 1) * P], y_tok[:, q, j * P:(j + 1) * P], ident)
                else:
                    i = int(kind[1])
                    if i == 0:
                        pe.wait_ge(gated, n_unit)
                    for q in range(2):
                        for k in range(KI):
                            tok = (2 * i + q) * P
                            m = nc.tensor.matmul(bank[:, q * DIM:(q + 1) * DIM], yg[:, k, tok:tok + P], w_out[:, k],
                                                 start=(k == 0), stop=(k == KI - 1))
                m.then_inc(made, 1)

            def sum_state(s, k, state0):
                if k == 0:
                    pe.wait_ge(hc_half, state0 * 2 + (s + 1 + RING) * 2)
                for q in range(T // P):
                    m = nc.tensor.matmul(y_ps[:, q, k * P:(k + 1) * P], hb[s % RING][:, k, q * P:(q + 1) * P], ident,
                                         is_transpose=True, start=False, stop=(s % DS == DS - 1),
                                         skip_group_check=True)
                if k == KI - 1:
                    m.then_inc(summed, 1)

            loads, proj_at = [None], [None]
            pe.wait_ge(sel_ld, 32)
            with pe.Fori(0, 2) as d:
                pe.wait_ge(w_ready, d + 1)
                base = d * DIR_PRODUCTS
                for k in range(KI):
                    pe.wait_ge(taken, base + (k if k else 1))
                    for i in range(KD):
                        m = nc.tensor.matmul(g_ps[:, k % 2, 0:DIM], op_t[:, i, k * P:(k + 1) * P], cw_t[:, i],
                                             start=(i == 0), stop=(i == KD - 1))
                    m.then_inc(made, 1)
                for k in range(KI):
                    m = nc.tensor.matmul(y_ps[:, k], ident, hb[0][:, k % 2], start=True, stop=False,
                                         skip_group_check=True)
                m.then_inc(summed, RING)
                loads[0] = d * (16 * (NCH + 1)) + 16
                proj_at[0] = FIRST_FRONT.index(("proj", None))
                for at, (kind, s) in enumerate(FIRST_FRONT):
                    make(kind, s, at, d * DIR_PRODUCTS + NW2, 0, d * FRONTS, None, 0)
                with pe.Fori(0, NCH) as ch:
                    for b in range(BATCH):
                        base = d * DIR_PRODUCTS + ch * (2 * NU) + (NW2 + NF + b * NU)
                        n_front = d * FRONTS + ch * 2 + (b + 1)
                        n_unit = d * (UNITS + 1) + ch * 2 + (b + 2)
                        loads[0] = d * (16 * (NCH + 1)) + ch * 16 + 16 * (b + 1)
                        proj_at[0] = AT["proj"]
                        at = 0

                        state0 = d * (UNITS * DS) + ch * (2 * DS) + b * DS
                        for s in range(DS):
                            todo = step_products(s)
                            if s == LAG:
                                pe.wait_ge(y_out, n_unit - 1)
                            for k in range(KI):
                                for _ in range(MAKE[k]):
                                    if todo:
                                        make(*todo.pop(0), at, base, 1 - b, n_front, n_unit, b)
                                        at += 1
                                if s == LAG:
                                    for q in range(T // P):
                                        nc.tensor.matmul(y_ps[:, q, k * P:(k + 1) * P], xs[:, k, q * P:(q + 1) * P],
                                                         skip_diag[:, k], start=(k == 0), stop=False,
                                                         skip_group_check=True)
                                sum_state(s - LAG, k, state0)
                for s in range(-LAG, 0):
                    for k in range(KI):
                        sum_state(s, k, (d + 1) * (UNITS * DS))
                base = d * DIR_PRODUCTS + (NW2 + NF + UNITS * NU)
                for at, (kind, s) in enumerate(TAIL):
                    make(kind, s, at, base, 0, None, d * (UNITS + 1) + (UNITS + 2), 0)

        @block.scalar
        def _(act):
            def take(kind, s, at, base, fb, n_front, state0):
                bank = product(kind, s, at)
                idx = base + (at + 1)
                if kind == "B":
                    act.wait_ge(bu_ready, state0 + (s + 1 + shift[0]))
                if kind == "C":
                    act.wait_ge(hc_half, state0 * 2 + (s + 1 + shift[0]) * 2)
                if kind == "c0":
                    act.wait_ge(u_ready, n_front + 1)
                if kind == "z0":
                    act.wait_ge(gated, n_unit_gate[0])
                if kind == "d0":
                    act.wait_ge(delta_ready, n_front + 1)
                if kind == "o0":
                    act.wait_ge(res_out, res_stores[0])
                act.wait_ge(made, idx)
                if kind == "B":
                    m = nc.scalar.activation(b_bc[s % RING], bank, ACT.Copy)
                elif kind == "C":
                    m = nc.scalar.activation(c_bc[s % RING], bank, ACT.Copy)
                elif kind[0] == "x":
                    j = int(kind[1])
                    m = nc.scalar.activation(x_pre[fb][:, j, PAD:PAD + T], bank, ACT.Copy)
                elif kind[0] == "c":
                    j = int(kind[1])
                    m = nc.scalar.activation(xs[:, j], bank, ACT.Identity, bias=conv_b[:, j:j + 1])
                elif kind[0] == "z":
                    if kind == "z3":
                        nc.scalar.activation(x_pre[fb][:, :, 0:PAD], x_pre[fb][:, :, T:T + PAD], ACT.Copy)
                    m = nc.scalar.activation(zs[fb][:, int(kind[1])], bank, ACT.Copy)
                elif kind == "proj":
                    m = nc.scalar.activation(proj[0:3 * W + DTR], bank[0:3 * W + DTR], ACT.Copy)
                elif kind[0] == "d":
                    j = int(kind[1])
                    m = nc.scalar.activation(dt_x[:, j], bank, ACT.Identity, bias=dt_b[:, j:j + 1])
                elif kind[0] == "t":
                    m = nc.scalar.activation(yg[:, int(kind[1])], bank, ACT.Copy)
                else:
                    i = int(kind[1])
                    m = nc.scalar.activation(res[:, 2 * i:2 * i + 2].rearrange("p q n -> p (q n)"), bank, ACT.Copy)
                m.then_inc(taken, 1)
                if kind == "proj":
                    act.wait_ge(taken, idx + 1)
                    nc.scalar.activation(parts[fb][0:3 * W], proj[0:3 * W], ACT.Copy).then_inc(split_act, 1)

            def take_sums(sums):
                act.wait_ge(summed, sums)
                nc.scalar.activation(y_tok, y_ps[:, :, :], ACT.Copy).then_inc(y_out, 1)

            def silus(fb, idx):
                act.wait_ge(taken, idx)
                nc.scalar.activation(xs, xs, ACT.Silu).then_inc(silu_done, 1)
                nc.scalar.activation(zs[fb], zs[fb], ACT.Silu).then_inc(silu_done, 1)
                nc.scalar.preload_act_table_set("natural_log_exp_and_others")

            def split(i, fb, n_front):
                rows = (2 - i) * W
                act.wait_ge(split_dve, n_front * 2 + (i + 1))
                nc.scalar.activation(parts[fb][0:rows], rest[0:rows], ACT.Copy).then_inc(split_act, 1)

            def softplus(i, fb, n_front, idx):
                if i == 0:
                    act.wait_ge(taken, idx)
                    nc.scalar.activation(delta[fb], dt_x, ACT.Relu, scale=-1.0, bias=clip).then_inc(soft, 1)
                elif i == 1:
                    act.wait_ge(soft, n_front * 3 + 1)
                    nc.scalar.activation(delta[fb], delta[fb], ACT.Exp, scale=-1.0, bias=clip).then_inc(soft, 1)
                else:
                    act.wait_ge(soft, n_front * 3 + 2)
                    nc.scalar.activation(delta[fb], delta[fb], ACT.Ln, bias=1.0).then_inc(soft, 1)

            n_unit_gate, res_stores, shift = [None], [None], [0]
            with act.Fori(0, 2) as d:
                act.wait_ge(w_ld, d * (16 * 9) + 16 * 9)
                nc.scalar.activation(a_exp, a_log, ACT.Exp).then_inc(a_exped, 1)
                base = d * DIR_PRODUCTS
                for k in range(KI):
                    act.wait_ge(made, base + (k + 1))
                    nc.scalar.activation(w_out[:, k], g_ps[:, k % 2, 0:DIM], ACT.Copy).then_inc(taken, 1)
                base = d * DIR_PRODUCTS + NW2
                n_front = d * FRONTS
                n_unit_gate[0] = d * (UNITS + 1) + 1
                shift[0] = -DS
                for at, (kind, s) in enumerate(FIRST_FRONT):
                    take(kind, s, at, base, 0, n_front, d * (UNITS * DS))
                    if kind == "z3":
                        silus(0, base + at + 2)
                    if kind == "proj":
                        split(0, 0, n_front)
                        split(1, 0, n_front)
                    if kind == "d3":
                        softplus(0, 0, n_front, base + at + 2)
                        softplus(1, 0, n_front, None)
                        softplus(2, 0, n_front, None)
                shift[0] = 0
                with act.Fori(0, NCH) as ch:
                    for b in range(BATCH):
                        fb = 1 - b
                        base = d * DIR_PRODUCTS + ch * (2 * NU) + (NW2 + NF + b * NU)
                        n_front = d * FRONTS + ch * 2 + (b + 1)
                        state0 = d * (UNITS * DS) + ch * (2 * DS) + b * DS
                        exp0 = d * (UNITS * DS * KI) + ch * (2 * DS * KI) + b * DS * KI
                        n_unit_gate[0] = d * (UNITS + 1) + ch * 2 + (b + 2)
                        res_stores[0] = d * (16 * SLOTS) + ch * 32 + (16 * b + 16)
                        at = 0
                        act.wait_ge(delta_ready, d * FRONTS + ch * 2 + (b + 2))
                        for s in range(DS):
                            todo = step_products(s)
                            for k in range(KI):
                                act.wait_ge(scanned, exp0 + (s * KI + k + 1))
                                nc.scalar.activation(da_ps[:, k % 2], delta[b][:, k], ACT.Exp,
                                                     scale=a_neg[:, k, s:s + 1]).then_inc(da_ready, 1)
                                for _ in range(GRAB[k]):
                                    if not todo:
                                        break
                                    kind, a = todo.pop(0)
                                    take(kind, a, at, base, fb, n_front, state0)
                                    at += 1
                                    if kind == "z3":
                                        silus(fb, base + at + 1)
                                    if kind == "d3":
                                        last_dt = base + at + 1
                            if s == LAG - 1:
                                take_sums(d * DIR_SUMS + ch * (2 * DS) + (b * DS + LAG + RING))
                            if s == 10:
                                split(0, fb, n_front)
                            if s == 12:
                                split(1, fb, n_front)
                            if s == 11:
                                softplus(0, fb, n_front, last_dt)
                                softplus(1, fb, n_front, None)
                            if s == 12:
                                softplus(2, fb, n_front, None)
                base = d * DIR_PRODUCTS + (NW2 + NF + UNITS * NU)
                res_stores[0] = d * (16 * SLOTS) + (16 * UNITS + 16)
                take_sums((d + 1) * DIR_SUMS)
                for at, (kind, s) in enumerate(TAIL):
                    take(kind, s, at, base, 0, None, None)

        @block.gpsimd
        def _(pool):
            with pool.Fori(0, 2) as d:
                with pool.Fori(0, NCH) as ch:
                    for b in range(BATCH):
                        first = d * DIR_PRODUCTS + ch * (2 * NU) + (NW2 + NF + b * NU)
                        pool.wait_ge(u_ready, d * FRONTS + ch * 2 + (b + 2))
                        for s in range(DS):
                            pool.wait_ge(taken, first + (AT[f"B{s}"] + 2 if s >= 2 else 2 * s - 4 + 2))
                            pool.wait_ge(summed, d * DIR_SUMS + ch * (2 * DS) + (b * DS + s + LAG + 1))
                            nc.gpsimd.tensor_tensor(hb[s % RING], u[b],
                                                    b_bc[s % RING].unsqueeze(1).to_broadcast([P, KI, T]),
                                                    ALU.mult).then_inc(bu_ready, 1)

        @block.vector
        def _(dve):
            def leave_rest(i, fb, n_front):
                rows = (3 - 2 * i) * W
                dve.wait_ge(split_act, n_front * 3 + (i + 1))
                if i:
                    dve.wait_ge(split_dve, n_front * 2 + 1)
                nc.vector.tensor_tensor(rest[0:rows], (rest if i else proj)[0:rows], parts[fb][0:rows],
                                        ALU.subtract).then_inc(split_dve, 1)

            def delta_and_u(fb, n_front):
                dve.wait_ge(soft, n_front * 3 + 3)
                nc.vector.tensor_tensor(delta[fb], delta[fb], dt_x, ALU.max).then_inc(delta_ready, 1)
                dve.wait_ge(silu_done, n_front * 2 + 2)
                dve.wait_ge(delta_ready, n_front + 2)
                nc.vector.tensor_tensor(u[fb], delta[fb], xs, ALU.mult).then_inc(u_ready, 1)

            def gate(b, idx):
                dve.wait_ge(taken, idx)
                nc.vector.tensor_tensor(yg, yg, zs[b], ALU.mult).then_inc(gated, 1)

            nc.vector.memset(clip, SP_CLIP)
            for i, (s, n) in enumerate(((taken, 1), (gated, 1), (delta_ready, 1), (u_ready, 1), (bu_ready, RING), (hc_half, 2 * RING),
                                      (scanned, 2), (res_out, 16))):
                nc.vector.memset(hold[:, i:i + 1], 0.0).then_inc(s, n)
            nc.vector.memset(zs[1], 0.0)
            for i in range(2, RING):
                nc.vector.memset(hb[i], 0.0)
            nc.vector.memset(w_proj, 0.0).then_inc(w_zero, 1)
            with dve.Fori(0, 2) as d:
                dve.wait_ge(sel_ld, 32)
                dve.wait_ge(w_ld, d * (16 * 9) + 16 * 9)
                for k in range(KI):
                    for a in range(TAPS):
                        nc.vector.tensor_scalar(conv_diag[:, k, a], ident, conv_w[:, k, a:a + 1], None, ALU.mult)
                    nc.vector.tensor_scalar(skip_diag[:, k], ident, d_skip[:, k:k + 1], None, ALU.mult)
                for b in range(BATCH):
                    nc.vector.memset(x_pre[b], 0.0)
                    nc.vector.memset(state[b], 0.0)
                dve.wait_ge(a_exped, d + 1)
                nc.vector.tensor_scalar(a_neg.rearrange("p k s -> p (k s)"), a_exp, -1.0, None,
                                        ALU.mult).then_inc(saved, 1)
                dve.wait_ge(saved, d * (UNITS * DS + 1) + 1)
                nc.vector.memset(rest, 0.0).then_inc(w_ready, 1)
                leave_rest(0, 0, d * FRONTS)
                leave_rest(1, 0, d * FRONTS)
                delta_and_u(0, d * FRONTS)
                with dve.Fori(0, NCH) as ch:
                    for b in range(BATCH):
                        first = d * DIR_PRODUCTS + ch * (2 * NU) + (NW2 + NF + b * NU)
                        state0 = d * (UNITS * DS) + ch * (2 * DS) + b * DS
                        exp0 = d * (UNITS * DS * KI) + ch * (2 * DS * KI) + b * DS * KI
                        n_front = d * FRONTS + ch * 2 + (b + 1)

                        def save(s):
                            dve.wait_ge(scanned, exp0 + (s * KI + KI + 2))
                            nc.vector.tensor_copy(state[b][:, s], hb[s % RING][:, :, T - 1]).then_inc(saved, 1)

                        def times_c(s, half):
                            h = hb[s % RING][:, half * (KI // 2):(half + 1) * (KI // 2)]
                            dve.wait_ge(saved, saved0 + (s + 2))
                            dve.wait_ge(taken, first + (AT[f"C{s}"] + 2 if s >= 2 else 2 * s - 4 + 3))
                            nc.vector.tensor_tensor(h, h, c_bc[s % RING].unsqueeze(1).to_broadcast([P, KI // 2, T]),
                                                    ALU.mult).then_inc(hc_half, 1)

                        saved0 = d * (UNITS * DS + 1) + ch * (2 * DS) + b * DS
                        dve.wait_ge(saved, saved0 + 1)
                        for s in range(DS):
                            dve.wait_ge(bu_ready, state0 + (s + 1 + RING))
                            for k in range(KI):
                                if s and k == 1:
                                    save(s - 1)
                                if s and k == 2:
                                    times_c(s - 1, 0)
                                dve.wait_ge(da_ready, exp0 + (s * KI + k + 1))
                                nc.vector.tensor_tensor_scan(hb[s % RING][:, k], da_ps[:, k % 2], hb[s % RING][:, k],
                                                             state[b][:, s, k:k + 1], ALU.mult, ALU.add
                                                             ).then_inc(scanned, 1)
                            if s:
                                times_c(s - 1, 1)
                            if s == 3:
                                gate(1 - b, first + (AT["t3"] + 2))
                            if s == 9:
                                leave_rest(0, 1 - b, n_front)
                            if s == 11:
                                leave_rest(1, 1 - b, n_front)
                            if s == 13:
                                delta_and_u(1 - b, n_front)
                        save(DS - 1)
                        times_c(DS - 1, 0)
                        times_c(DS - 1, 1)
                gate(1, d * DIR_PRODUCTS + (NW2 + NF + UNITS * NU + TAIL.index(("t3", None)) + 2))


def epilogue(nc, t, arena, y_ps, tok_scr, rows, perm, sem):
    c = Carve(arena)
    bias = c.take(BC)
    hold = c.take(4)
    out_sb = c.take(2 * BC).rearrange("p (i n) -> p i n", i=2)
    got = c.take(4 * BC).rearrange("p (i d n) -> p i d n", i=2, d=2)
    res_sb = c.take(2 * NT * BC).rearrange("p (j n) -> p j n", j=2 * NT)
    NB = 4
    d_sb = c.take(NB * NT * P // 2).rearrange("p (i j n) -> p i j n", i=NB, j=NT // 2)
    bias_ld, res_ld, d_ld = sem("bias_ld"), sem("res_ld"), [sem(f"d_ld{i}") for i in range(NB)]
    d_used, out_ready, out_st = sem("d_used"), sem("out_ready"), [sem("out_st0"), sem("out_st1")]
    got_ld, added = [sem("got_ld0"), sem("got_ld1")], sem("added")

    with nc.Block() as block:
        @block.sync
        def _(sp):
            sp.dma_start(bias, t["bias"].to_broadcast([P, BC])).then_inc(bias_ld, 16)
            gathered = sp.value_load(perm[0:1, 1:2], min_val=0, max_val=1)
            with sp.If(gathered == 0):
                for h in range(NB):
                    sp.dma_start(d_sb[:, h], t["despiral"][0, h]).then_inc(d_ld[h], 16)
                with sp.Fori(0, NT - 1) as i:
                    for h in range(NB):
                        nxt = sp.snap(i + 1)
                        sp.wait_ge(d_used, i * NB + (h + 1))
                        sp.dma_start(d_sb[:, h], t["despiral"][nxt, h]).then_inc(d_ld[h], 16)

        @block.gpsimd
        def _(pool):
            gathered = pool.value_load(perm[0:1, 1:2], min_val=0, max_val=1)
            with pool.If(gathered == 1):
                for i in range(NT):
                    if i >= 2:
                        pool.wait_ge(added, i - 1)
                    for d in range(2):
                        at = (1 + d) * NT + i
                        pool.indirect_dma_start(got[:, i % 2, d], None, tok_scr,
                                                bass.IndirectOffsetOnAxis(ap=rows[:, at:at + 1], axis=0)
                                                ).then_inc(got_ld[i % 2], 16)

        @block.scalar
        def _(act):
            gathered = act.value_load(perm[0:1, 1:2], min_val=0, max_val=1)
            with act.If(gathered == 0):
                for d in range(2):
                    for ch in range(NCH):
                        at = d * ROWS + (ch + 1) * T
                        j = (d * NCH + ch) * (T // P)
                        act.dma_start(res_sb[:, j:j + T // P],
                                      tok_scr[at:at + T].rearrange("(q p) n -> p q n", p=P)).then_inc(res_ld, 16)
            with act.Fori(0, NT // 2) as i:
                for q in range(2):
                    row = act.snap(i * (2 * P) + q * P)
                    act.wait_ge(out_ready, i * 2 + (q + 3))
                    act.dma_start(t["out"][bass.ds(row, P), :], out_sb[:, q]).then_inc(out_st[q], 16)
            for q in range(2):
                act.wait_ge(out_st[q], 16 * (NT // 2 + 1))

        @block.tensor
        def _(pe):
            gathered = pe.value_load(perm[0:1, 1:2], min_val=0, max_val=1)
            with pe.If(gathered == 0):
                pe.wait_ge(res_ld, 16 * 2 * NCH)
                with pe.Fori(0, NT // 2) as i:
                    for q in range(2):
                        pe.wait_ge(out_ready, i * 2 + (q + 1))
                        for h in range(NB):
                            pe.wait_ge(d_ld[h], i * 32 + 16 * (q + 1))
                            for j in range(NT // 2):
                                k = h * (NT // 2) + j
                                m = nc.tensor.matmul(y_ps[:, q], d_sb[:, h, j], res_sb[:, k],
                                                     start=(k == 0), stop=(k == 2 * NT - 1))
                            m.then_inc(d_used, 1)

        @block.vector
        def _(dve):
            dve.wait_ge(bias_ld, 16)
            for q in range(2):
                nc.vector.memset(hold[:, q:q + 1], 0.0).then_inc(out_st[q], 16)
                nc.vector.memset(hold[:, q + 2:q + 3], 0.0).then_inc(out_ready, 1)
            gathered = dve.value_load(perm[0:1, 1:2], min_val=0, max_val=1)
            with dve.If(gathered == 1):
                with dve.Fori(0, NT // 2) as i:
                    for q in range(2):
                        dve.wait_ge(got_ld[q], i * 32 + 32)
                        dve.wait_ge(out_st[q], i * 16 + 16)
                        nc.vector.tensor_tensor(out_sb[:, q], got[:, q, 0], got[:, q, 1], ALU.add).then_inc(added, 1)
                        dve.wait_ge(added, i * 2 + (q + 1))
                        nc.vector.tensor_tensor(out_sb[:, q], out_sb[:, q], bias, ALU.add).then_inc(out_ready, 1)
            with dve.Else():
                with dve.Fori(0, NT // 2) as i:
                    for q in range(2):
                        dve.wait_ge(d_used, i * (2 * NB) + NB * (q + 1))
                        dve.wait_ge(out_st[q], i * 16 + 16)
                        nc.vector.tensor_tensor(out_sb[:, q], y_ps[:, q], bias, ALU.add).then_inc(out_ready, 1)


def kernel(**inputs):
    import numpy as np
    import concourse.bacc as bacc
    from concourse.bass_utils import run_bass_kernel_spmd

    def blocks(a):
        return a.reshape(-1, P, a.shape[-1]).transpose(1, 0, 2)

    def both(f):
        return np.stack([f("m1"), f("m2")])

    v = {k[len("L0_conv_"):] if k != "x" else k: np.asarray(a) for k, a in inputs.items()}
    bf16 = mybir.dt.np(BF16)
    ds = {
        "x": v["x"].reshape(BATCH, DIM, NT, P).transpose(3, 2, 0, 1).reshape(P, NT, BC),
        "spiral": np.concatenate([v["spiral_eye"], v["spiral_eye"][:2 * P]]).reshape(NT + 2, P, NT, P).transpose(0, 3, 2, 1),
        "despiral": np.stack([v[k].reshape(NT, P, 2, NT // 2, P).transpose(0, 2, 4, 3, 1)
                              for k in ("despiral_eye", "despiral_r_eye")], 1).reshape(NT, 4, P, NT // 2, P),
        "x_tok": v["x"].reshape(BC, L).T,
        "eyes": np.concatenate([v["spiral_eye"], v["despiral_eye"], v["despiral_r_eye"]]).reshape(3 * NT, P, L),
        "iota": (MARK + np.arange(L, dtype=np.float32))[None],
        "ln": np.concatenate([v["ln_gamma"].reshape(KD, P).T, v["ln_beta"].reshape(KD, P).T], 1),
        "ident": np.eye(P, dtype=np.float32),
        "rev": np.eye(P, dtype=np.float32)[::-1],
        "sel": np.repeat(np.tile(np.eye(2 * DS, dtype=np.float32), (3, 1))[:, :, None], P, 2).astype(bf16),
        "in_proj": both(lambda m: blocks(v[m + "_in_proj"])),
        "small": both(lambda m: np.concatenate([
            blocks(v[m + "_conv_w"]).reshape(P, -1), v[m + "_conv_b"].reshape(KI, P).T,
            v[m + "_dt_b"].reshape(KI, P).T, v[m + "_D"].reshape(KI, P).T,
            blocks(v[m + "_A_log"]).reshape(P, -1)], 1)),
        "x_proj": both(lambda m: blocks(v[m + "_x_proj"])),
        "dt_w": both(lambda m: v[m + "_dt_w"]),
        "out_proj": both(lambda m: blocks(v[m + "_out_proj"].T)),
        "conv_w": np.stack([blocks(v["conv_w"][:, h * DIM:(h + 1) * DIM].T) for h in range(2)]),
        "bias": np.concatenate([v["conv_b"]] * BATCH)[None],
    }
    nc = bacc.Bacc("TRN2", target_bir_lowering=False, num_devices=1)
    arrays, aps = {}, {}
    for k, a in ds.items():
        arrays[k + "_dram"] = np.ascontiguousarray(a)
        aps[k] = nc.dram_tensor(k + "_dram", a.shape, mybir.dt.from_np(a.dtype), kind="ExternalInput").ap()
    aps["out"] = nc.dram_tensor("out_dram", (L, BC), F32, kind="ExternalOutput").ap()
    build(nc, aps)
    r = run_bass_kernel_spmd(nc, [arrays], core_ids=[0])
    out = r.results[0]["out_dram"]
    return out.reshape(L, BATCH, DIM).transpose(1, 2, 0).reshape(BATCH, DIM, 64, 64)
```
